# Optimizing a Trainium2 kernel written in Bass

```python
import numpy as np
import jax
import jax.numpy as jnp

def _softmax(x, axis=-1):
    return jax.nn.softmax(x, axis=axis)
def _gelu(x):
    return jax.nn.gelu(x, approximate=True)
def _silu(x):
    return jax.nn.silu(x)
def _sigmoid(x):
    return jax.nn.sigmoid(x)
def _layernorm(x, axis=-1, eps=1e-5):
    m = jnp.mean(x, axis=axis, keepdims=True)
    v = jnp.var(x, axis=axis, keepdims=True)
    return (x - m) / jnp.sqrt(v + eps)
def _scatter_add(tgt, idx, src, axis=0):
    return tgt.at[idx].add(src)
def _segment_sum(src, seg, n):
    return jax.ops.segment_sum(src, seg, n)

kernel_name = 'mk_adj_resnorm_d1_adj_512_e4be7f'

def setup_inputs(seed: int = 0):
    np.random.seed(seed)
    _w = jnp.asarray
    def _rec_inputs():
        import jax
        import jax.numpy as jnp
        _gk = jax.random.key(seed)
        x = 7.22e-05 + 1 * jax.random.normal(jax.random.fold_in(_gk, 1), (16, 1024, 512), jnp.float32)
        _a = jax.random.bernoulli(jax.random.fold_in(_gk, 2), 0.015625, (1024, 1024))
        _a = jnp.logical_or(_a, jnp.swapaxes(_a, -1, -2))
        _a = jnp.logical_or(_a, jnp.eye(1024, dtype=bool))
        _af = _a.astype(jnp.float32)
        adj = _af
        return x, adj
    x, adj = _rec_inputs()
    def _L0_gnn_setup():
        import jax, jax.numpy as jnp
        import numpy as np
        B, N, D = (8, 2048, 512)
        key = jax.random.key(seed)
        k1, k2, k3, k4, k5 = jax.random.split(key, 5)
        neuron_states = jax.random.normal(k1, (B, N, D), dtype=jnp.float32)
        adjacency = jax.random.randint(k2, (N, N), 0, 2).astype(jnp.float32)
        scale = 1.0 / np.sqrt(D)
        Wq = jax.random.normal(k3, (D, D), dtype=jnp.float32) * scale
        Wk = jax.random.normal(k4, (D, D), dtype=jnp.float32) * scale
        Wv = jax.random.normal(k5, (D, D), dtype=jnp.float32) * scale
        return {'neuron_states': neuron_states, 'adjacency': adjacency, 'Wq': Wq, 'Wk': Wk, 'Wv': Wv}
    _L0_gnn_all = _L0_gnn_setup()
    _L0_gnn_in = {k: v for k, v in _L0_gnn_all.items() if k in ('Wq', 'Wk', 'Wv', )}
    del _L0_gnn_all

    return {
        "x": x,
        "adj": adj,
        "L0_gnn_Wq": _L0_gnn_in["Wq"],
        "L0_gnn_Wk": _L0_gnn_in["Wk"],
        "L0_gnn_Wv": _L0_gnn_in["Wv"],
    }

def reference(x, adj, L0_gnn_Wq, L0_gnn_Wk, L0_gnn_Wv):
    import jax
    import jax.numpy as jnp
    def _L0_gnn_ref(neuron_states, adjacency, Wq, Wk, Wv):
        import jax, jax.numpy as jnp
        import numpy as np
        B, N, D = (8, 2048, 512)
        q = jnp.einsum('bnd,ed->bne', neuron_states, Wq)
        k = jnp.einsum('bnd,ed->bne', neuron_states, Wk)
        v = jnp.einsum('bnd,ed->bne', neuron_states, Wv)
        rel = jnp.einsum('bnd,bmd->bnm', q, k)
        rel = adjacency.T[None, :, :] * rel
        rel = rel / jnp.linalg.norm(rel, axis=2, keepdims=True)
        return jnp.einsum('bnm,bmd->bnd', rel, v)

    x = _layernorm(x + _L0_gnn_ref(x, adj, L0_gnn_Wq, L0_gnn_Wk, L0_gnn_Wv), axis=-1)
    return x


_drawn_inputs = setup_inputs


def setup_inputs(seed=0):
    import zlib

    import numpy as np

    out = dict(_drawn_inputs(seed))
    spreads = {}
    factors = {}
    for name, (base, spread) in spreads.items():
        noise = np.random.default_rng([zlib.crc32(name.encode()), seed]).standard_normal(out[name].shape)
        drawn = base * np.exp(spread * noise) if base else spread * noise
        out[name] = jnp.asarray(drawn.astype(out[name].dtype))
    for name, factor in factors.items():
        out[name] = (out[name] * factor).astype(out[name].dtype)
    return out
```

```python
from contextlib import ExitStack

import concourse.bass as bass
from concourse import mybir

F32 = mybir.dt.float32
F32R = mybir.dt.float32r
ALU = mybir.AluOpType
ACT = mybir.ActivationFunctionType

P = 128
BANK = 512
DMA = 16
EPS = 1e-5


def adjacency_attention_layernorm(nc, x, xT, adj, wq, wk, wvT, out):
    B, N, D = x.shape
    KD = D // P
    MT = N // P
    HALVES = N // BANK
    QT = BANK // P
    assert D == BANK and HALVES == 2 and KD == QT == 4

    FIRST_GROUPS = KD + KD + MT
    GROUPS = KD + QT + KD + QT + MT
    Y1, O0, Y0, O1, V = 0, KD, KD + QT, 2 * KD + QT, 2 * KD + 2 * QT
    SPLITS = KD + KD + MT
    SPLIT_Y1, SPLIT_Y0, SPLIT_V = 0, KD, 2 * KD
    O1_LAST = Y0
    SCORES = HALVES * MT
    PIECES = HALVES * KD
    TILES = HALVES * QT
    RING = 3
    SRING = 4
    MRING = 2
    SQRING = 2
    assert GROUPS % RING == 0 and SCORES % SRING == 0

    with ExitStack() as ctx:
        def sb(name, shape, dt):
            return ctx.enter_context(nc.sbuf_tensor(name, shape, dt))

        def sem(name):
            return ctx.enter_context(nc.semaphore(name))

        x_hi = sb("x_hi", [P, KD, N], F32R)
        x_lo = sb("x_lo", [P, KD, N], F32R)
        x_raw = sb("x_raw", [P, KD, BANK], F32)
        a_hi = sb("a_hi", [P, KD, D], F32R)
        a_lo = sb("a_lo", [P, KD, D], F32R)
        wv_hi = sb("wv_hi", [P, KD, D], F32R)
        wv_lo = sb("wv_lo", [P, KD, D], F32R)
        y_hi = sb("y_hi", [P, KD, BANK], F32R)
        y_lo = sb("y_lo", [P, KD, BANK], F32R)
        v_hi = sb("v_hi", [P, MT, D], F32R)
        v_lo = sb("v_lo", [P, MT, D], F32R)
        rel_hi = sb("rel_hi", [P, MT, BANK], F32R)
        rel_lo = sb("rel_lo", [P, MT, BANK], F32R)
        adj_sb = sb("adj_sb", [P, MT, N], F32)
        masked = sb("masked", [P, MRING, BANK], F32)
        squares = sb("squares", [P, SQRING, BANK], F32)
        square_sum = sb("square_sum", [P, HALVES, BANK], F32)
        res = sb("res", [P, QT, D], F32)
        ones = sb("ones", [P, 1], F32)
        minus_half = sb("minus_half", [P, QT], F32)
        norm2 = sb("norm2", [P, QT], F32)
        rnorm = sb("rnorm", [P, QT], F32)
        stats = sb("stats", [P, 6], F32)
        mean_var = sb("mean_var", [P, 2], F32)
        var_eps = sb("var_eps", [P, 1], F32)
        rstd = sb("rstd", [P, 1], F32)

        ring = [ctx.enter_context(nc.psum_tensor(f"ring{i}", [P, BANK], F32)) for i in range(RING)]
        score = [ctx.enter_context(nc.psum_tensor(f"score{i}", [P, BANK], F32)) for i in range(SRING)]
        norm_ps = ctx.enter_context(nc.psum_tensor("norm_ps", [P, BANK], F32))

        wq_loaded = sem("wq_loaded")
        wk_loaded = sem("wk_loaded")
        wv_loaded = sem("wv_loaded")
        x_loaded = sem("x_loaded")
        adj_loaded = [sem(f"adj_loaded{h}") for h in range(HALVES)]
        res_loaded = sem("res_loaded")
        out_stored = sem("out_stored")
        const_set = sem("const_set")
        w_hi_made = sem("w_hi_made")
        w_split = sem("w_split")
        x_hi_made = sem("x_hi_made")
        x_split = sem("x_split")
        group_done = sem("group_done")
        group_hi_made = sem("group_hi_made")
        group_taken = sem("group_taken")
        score_done = sem("score_done")
        score_masked = sem("score_masked")
        rel_hi_made = sem("rel_hi_made")
        rel_split = sem("rel_split")
        squared = sem("squared")
        square_added = sem("square_added")
        norm2_done = sem("norm2_done")
        norm2_copied = sem("norm2_copied")
        rnorm_made = sem("rnorm_made")
        mean_var_made = sem("mean_var_made")
        var_made = sem("var_made")
        rstd_made = sem("rstd_made")
        normed = sem("normed")

        w_stage = adj_sb[:, :, :].rearrange("p m (a n) -> p (m a) n", n=BANK)
        wq_raw, wk_raw, wv_raw = (w_stage[:, KD * i:KD * (i + 1), :] for i in range(3))
        wq_hi, wq_lo = rel_hi[:, 0:KD, :], rel_lo[:, 0:KD, :]
        wk_hi, wk_lo = rel_hi[:, KD:2 * KD, :], rel_lo[:, KD:2 * KD, :]
        weights = [(wq_raw, wq_hi, wq_lo), (wk_raw, wk_hi, wk_lo), (wv_raw, wv_hi, wv_lo)]
        w_loaded = [wq_loaded, wk_loaded, wv_loaded]

        xT_v = xT.rearrange("b (k p) n -> b p k n", p=P)
        x_v = x.rearrange("b (t p) d -> b p t d", p=P)
        out_v = out.rearrange("b (t p) d -> b p t d", p=P)
        adj_v = adj.rearrange("(m p) n -> p m n", p=P)

        def w_v(w):
            return w.rearrange("(k p) d -> p k d", p=P)

        def half(h):
            return slice(h * BANK, (h + 1) * BANK)

        def group_index(b, g):
            return b * GROUPS + (FIRST_GROUPS + g)

        def added_before(b, h):
            return b * (HALVES * (MT - 1)) + (h + 1) * (MT - 1)

        def bank(g):
            return ring[(FIRST_GROUPS + g) % RING]

        block = ctx.enter_context(nc.Block())

        @block.sync
        def _(sp):
            sp.dma_start(wq_raw, w_v(wq)).then_inc(wq_loaded, DMA)
            sp.dma_start(wk_raw, w_v(wk)).then_inc(wk_loaded, DMA)
            sp.dma_start(x_raw[:, :, :], xT_v[0, :, :, half(0)]).then_inc(x_loaded, DMA)
            sp.dma_start(wv_raw, w_v(wvT)).then_inc(wv_loaded, DMA)
            sp.wait_ge(x_split, KD)
            sp.dma_start(x_raw[:, :, :], xT_v[0, :, :, half(1)]).then_inc(x_loaded, DMA)
            sp.wait_ge(w_split, 3 * KD)
            for h in range(HALVES):
                sp.dma_start(adj_sb[:, :, half(h)], adj_v[:, :, half(h)]).then_inc(adj_loaded[h], DMA)

            def load_x(b, h):
                sp.wait_ge(x_split, b * PIECES + h * KD)
                sp.dma_start(x_raw[:, :, :], xT_v[b, :, :, half(h)]).then_inc(x_loaded, DMA)

            def load_res(b, h):
                sp.dma_start(res[:, :, :], x_v[b, :, h * QT:(h + 1) * QT, :]).then_inc(res_loaded, DMA)

            def store(b, h):
                for t in range(QT):
                    sp.wait_ge(normed, b * TILES + (h * QT + t + 1))
                    sp.dma_start(out_v[b, :, h * QT + t, :], res[:, t, :]).then_inc(out_stored, DMA)
                sp.wait_ge(out_stored, b * (TILES * DMA) + (h + 1) * QT * DMA)

            def batch(b, last):
                if not last:
                    load_x(b + 1, 0)
                store(b, 0)
                load_res(b, 1)
                if not last:
                    load_x(b + 1, 1)
                store(b, 1)
                if not last:
                    load_res(b + 1, 0)

            load_res(0, 0)
            with sp.Fori(0, B - 1) as b:
                batch(b, False)
            batch(B - 1, True)

        @block.tensor
        def _(pe):
            def product(bank_ap, pairs):
                for i, ((l_hi, l_lo), (r_hi, r_lo)) in enumerate(pairs):
                    pe.matmul(bank_ap, l_hi, r_hi, start=(i == 0), stop=False)
                    pe.matmul(bank_ap, l_hi, r_lo, start=False, stop=False)
                    mm = pe.matmul(bank_ap, l_lo, r_hi, start=False, stop=(i == len(pairs) - 1))
                return mm

            def tile_of(hi, lo, k, cols):
                return hi[:, k, cols], lo[:, k, cols]

            def cols(i):
                return slice(i * P, (i + 1) * P)

            def y_group(j, h, bank_ap):
                return product(bank_ap, [(tile_of(a_hi, a_lo, k, cols(j)), tile_of(x_hi, x_lo, k, half(h)))
                                         for k in range(KD)])

            def v_group(m, bank_ap):
                return product(bank_ap, [(tile_of(x_hi, x_lo, k, cols(m)), tile_of(wv_hi, wv_lo, k, slice(0, D)))
                                         for k in range(KD)])

            for j in range(KD):
                if j == 0:
                    pe.wait_ge(w_split, 2 * KD)
                if j >= RING:
                    pe.wait_ge(group_taken, j - RING + 1)
                product(ring[j % RING][:], [((wq_hi[:, k, cols(j)], wq_lo[:, k, cols(j)]),
                                             (wk_hi[:, k, :], wk_lo[:, k, :])) for k in range(KD)]
                        ).then_inc(group_done, 1)
            pe.wait_ge(x_split, KD)
            pe.wait_ge(group_taken, KD)
            for j in range(KD):
                g = KD + j
                pe.wait_ge(group_taken, g - RING + 1)
                y_group(j, 0, ring[g % RING][:]).then_inc(group_done, 1)
            pe.wait_ge(w_split, 3 * KD)
            for m in range(MT):
                g = 2 * KD + m
                if m == QT:
                    pe.wait_ge(x_split, PIECES)
                pe.wait_ge(group_taken, g - RING + 1)
                v_group(m, ring[g % RING][:]).then_inc(group_done, 1)
            pe.wait_ge(const_set, 2)

            def free_bank(b, g):
                pe.wait_ge(group_taken, group_index(b, g) - RING + 1)

            def scores(b, h):
                for i in range(MT):
                    s = h * MT + i
                    pe.wait_ge(score_masked, b * SCORES + (s + 1))
                    product(score[s % SRING][:], [(tile_of(x_hi, x_lo, k, cols(i)), tile_of(y_hi, y_lo, k, slice(0, BANK)))
                                                  for k in range(KD)]).then_inc(score_done, 1)

            def norms(b, h):
                pe.wait_ge(square_added, added_before(b, h + 1))
                pe.wait_ge(norm2_copied, b * HALVES + (h + HALVES))
                for t in range(QT):
                    mm = pe.matmul(norm_ps[:, t:t + 1], square_sum[:, h, cols(t)], ones[:, :],
                                   start=True, stop=True)
                mm.then_inc(norm2_done, 1)

            def outputs(b, h, g0):
                for t in range(QT):
                    free_bank(b, g0 + t)
                    pairs = [(tile_of(rel_hi, rel_lo, m, cols(t)), tile_of(v_hi, v_lo, m, slice(0, D)))
                             for m in range(MT)]
                    if t == 0:
                        pe.wait_ge(rel_split, b * SCORES + ((h + 1) * MT + MRING))
                    product(bank(g0 + t)[:], pairs).then_inc(group_done, 1)
                    if t == 0:
                        norms(b, h)

            def batch(b, last):
                pe.wait_ge(group_taken, group_index(b, 0))
                scores(b, 0)
                for j in range(KD):
                    free_bank(b, Y1 + j)
                    y_group(j, 1, bank(Y1 + j)[:]).then_inc(group_done, 1)
                outputs(b, 0, O0)
                pe.wait_ge(group_taken, group_index(b, Y1 + KD))
                scores(b, 1)
                if not last:
                    for j in range(KD):
                        if j == 0:
                            pe.wait_ge(x_split, (b + 1) * PIECES + KD)
                        free_bank(b, Y0 + j)
                        y_group(j, 0, bank(Y0 + j)[:]).then_inc(group_done, 1)
                outputs(b, 1, O1 if not last else O1_LAST)
                if not last:
                    for m in range(MT):
                        if m == QT:
                            pe.wait_ge(x_split, (b + 2) * PIECES)
                        free_bank(b, V + m)
                        v_group(m, bank(V + m)[:]).then_inc(group_done, 1)

            with pe.Fori(0, B - 1) as b:
                batch(b, False)
            batch(B - 1, True)

        @block.scalar
        def _(act):
            def x_piece(b, h, k):
                if k == 0:
                    act.wait_ge(x_loaded, b * (HALVES * DMA) + (h + 1) * DMA)
                act.activation(x_hi[:, k, half(h)], x_raw[:, k, :], ACT.Copy).then_inc(x_hi_made, 1)

            def group(ap_hi, g_index, bank_ap):
                act.wait_ge(group_done, g_index + 1)
                act.activation(ap_hi, bank_ap[:], ACT.Copy).then_inc(group_hi_made, 1)

            for w in (0, 1):
                act.wait_ge(w_loaded[w], DMA)
                for k in range(KD):
                    act.activation(weights[w][1][:, k, :], weights[w][0][:, k, :], ACT.Copy).then_inc(w_hi_made, 1)
            for k in range(KD):
                x_piece(0, 0, k)
            act.wait_ge(wv_loaded, DMA)
            for k in range(KD):
                act.activation(wv_hi[:, k, :], wv_raw[:, k, :], ACT.Copy).then_inc(w_hi_made, 1)
            for j in range(KD):
                group(a_hi[:, j, :], j, ring[j % RING])
            for j in range(KD):
                group(y_hi[:, j, :], KD + j, ring[(KD + j) % RING])
            for k in range(KD):
                x_piece(0, 1, k)
            for m in range(MT):
                group(v_hi[:, m, :], 2 * KD + m, ring[(2 * KD + m) % RING])

            def scores(b, h, last):
                for i in range(MT):
                    s = h * MT + i
                    act.wait_ge(score_masked, b * SCORES + (s + 1 + SRING))
                    act.activation(rel_hi[:, i, :], masked[:, s % MRING, :], ACT.Copy).then_inc(rel_hi_made, 1)
                    if i == 0:
                        act.wait_ge(norm2_copied, b * HALVES + (h + 1))
                        sq = square_sum[:, h, :]
                    else:
                        act.wait_ge(square_added, added_before(b, h) + max(i - SQRING, 0))
                        sq = squares[:, i % SQRING, :]
                    act.activation(sq, masked[:, s % MRING, :], ACT.Square).then_inc(squared, 1)
                    if h == 1 and not last and i >= KD:
                        x_piece(b + 1, 0, i - KD)

            def batch(b, last):
                scores(b, 0, last)
                for j in range(KD):
                    group(y_hi[:, j, :], group_index(b, Y1 + j), bank(Y1 + j))
                scores(b, 1, last)
                if not last:
                    for j in range(KD):
                        group(y_hi[:, j, :], group_index(b, Y0 + j), bank(Y0 + j))
                    for k in range(KD):
                        x_piece(b + 1, 1, k)
                    for m in range(MT):
                        group(v_hi[:, m, :], group_index(b, V + m), bank(V + m))

            with act.Fori(0, B - 1) as b:
                batch(b, False)
            batch(B - 1, True)

        @block.vector
        def _(dve):
            def split_weight(w):
                for k in range(KD):
                    raw, hi, lo = (a[:, k, :] for a in weights[w])
                    dve.wait_ge(w_hi_made, w * KD + k + 1)
                    dve.tensor_tensor(lo, raw, hi.bitcast(F32), ALU.subtract).then_inc(w_split, 1)

            def x_piece(b, h, k):
                dve.wait_ge(x_hi_made, b * PIECES + (h * KD + k + 1))
                dve.tensor_tensor(x_lo[:, k, half(h)], x_raw[:, k, :], x_hi[:, k, half(h)].bitcast(F32),
                                  ALU.subtract).then_inc(x_split, 1)

            def group(ap_hi, ap_lo, hi_count, bank_ap):
                dve.wait_ge(group_hi_made, hi_count)
                dve.tensor_tensor(ap_lo, bank_ap[:], ap_hi.bitcast(F32), ALU.subtract).then_inc(group_taken, 1)

            split_weight(0)
            split_weight(1)
            for k in range(KD):
                x_piece(0, 0, k)
            split_weight(2)
            for j in range(KD):
                group(a_hi[:, j, :], a_lo[:, j, :], j + 1, ring[j % RING])
            for j in range(KD):
                group(y_hi[:, j, :], y_lo[:, j, :], KD + j + 1, ring[(KD + j) % RING])
            for k in range(KD):
                x_piece(0, 1, k)
            for m in range(MT):
                group(v_hi[:, m, :], v_lo[:, m, :], 2 * KD + m + 1, ring[(2 * KD + m) % RING])

            def loop_group(b, ap_hi, ap_lo, split, g):
                group(ap_hi, ap_lo, b * SPLITS + (FIRST_GROUPS + split + 1), bank(g))

            def rest_of_scores(b, h, i):
                s = h * MT + i
                dve.wait_ge(rel_hi_made, b * SCORES + (s + 1))
                dve.tensor_tensor(rel_lo[:, i, :], masked[:, s % MRING, :], rel_hi[:, i, :].bitcast(F32),
                                  ALU.subtract).then_inc(rel_split, 1)

            def scores(b, h, last):
                dve.wait_ge(adj_loaded[h], DMA)
                for i in range(MT):
                    s = h * MT + i
                    dve.wait_ge(score_done, b * SCORES + (s + 1))
                    dve.wait_ge(squared, b * SCORES + (s + 1))
                    dve.wait_ge(rel_split, b * SCORES + (s + 1))
                    dve.tensor_tensor(masked[:, s % MRING, :], score[s % SRING][:], adj_sb[:, i, half(h)],
                                      ALU.mult).then_inc(score_masked, 1)
                    if i > 0:
                        rest_of_scores(b, h, i - 1)
                    if h == 1 and not last and i > KD:
                        x_piece(b + 1, 0, i - KD - 1)
                rest_of_scores(b, h, MT - 1)
                if h == 1 and not last:
                    x_piece(b + 1, 0, KD - 1)

            def outputs(b, h, g0, next_x):
                dve.wait_ge(norm2_done, b * HALVES + (h + 1))
                dve.tensor_copy(norm2[:, :], norm_ps[:, 0:QT]).then_inc(norm2_copied, 1)
                dve.wait_ge(res_loaded, b * (HALVES * DMA) + (h + 1) * DMA)
                dve.wait_ge(rnorm_made, b * HALVES + (h + 1))
                for t in range(QT):
                    tile = b * TILES + (h * QT + t)
                    dve.wait_ge(group_done, group_index(b, g0 + t + 1))
                    dve.scalar_tensor_tensor(out=res[:, t, :], in0=bank(g0 + t)[:], scalar=rnorm[:, t:t + 1],
                                             in1=res[:, t, :], op0=ALU.mult, op1=ALU.add).then_inc(group_taken, 1)
                    dve.wait_ge(group_taken, group_index(b, g0 + t + 1))
                    dve.bn_stats(stats[:, :], res[:, t, :])
                    dve.drain()
                    dve.bn_aggr(mean_var[:, :], stats[:, :]).then_inc(mean_var_made, 1)
                    dve.wait_ge(mean_var_made, tile + 1)
                    dve.tensor_scalar(var_eps[:, :], mean_var[:, 1:2], EPS, None, ALU.add).then_inc(var_made, 1)
                    dve.wait_ge(rstd_made, tile + 1)
                    dve.tensor_scalar(res[:, t, :], res[:, t, :], mean_var[:, 0:1], rstd[:, 0:1],
                                      ALU.subtract, ALU.mult).then_inc(normed, 1)
                    if next_x:
                        x_piece(b + 1, 1, t)

            def batch(b, last):
                scores(b, 0, last)
                for j in range(KD):
                    loop_group(b, y_hi[:, j, :], y_lo[:, j, :], SPLIT_Y1 + j, Y1 + j)
                outputs(b, 0, O0, False)
                scores(b, 1, last)
                if not last:
                    for j in range(KD):
                        loop_group(b, y_hi[:, j, :], y_lo[:, j, :], SPLIT_Y0 + j, Y0 + j)
                outputs(b, 1, O1 if not last else O1_LAST, not last)
                if not last:
                    for m in range(MT):
                        loop_group(b, v_hi[:, m, :], v_lo[:, m, :], SPLIT_V + m, V + m)

            with dve.Fori(0, B - 1) as b:
                batch(b, False)
            batch(B - 1, True)

        @block.gpsimd
        def _(pool):
            pool.memset(ones[:, :], 1.0).then_inc(const_set, 1)
            pool.memset(minus_half[:, :], -0.5).then_inc(const_set, 1)
            pool.sem_inc(score_masked, SRING)
            pool.sem_inc(squared, MRING)
            pool.sem_inc(rel_split, MRING)
            pool.sem_inc(square_added, MT - 1)
            pool.sem_inc(norm2_copied, HALVES)
            pool.wait_ge(const_set, 2)

            def sums(b, h):
                for i in range(1, MT):
                    pool.wait_ge(squared, b * SCORES + (h * MT + i + 1 + MRING))
                    pool.wait_ge(square_added, added_before(b, h) + (i - 1))
                    pool.tensor_tensor(square_sum[:, h, :], square_sum[:, h, :], squares[:, i % SQRING, :],
                                       ALU.add).then_inc(square_added, 1)

            def powers(b, h):
                pool.wait_ge(norm2_copied, b * HALVES + (h + 1 + HALVES))
                pool.tensor_tensor(rnorm[:, :], norm2[:, :], minus_half[:, :], ALU.pow).then_inc(rnorm_made, 1)
                for t in range(QT):
                    pool.wait_ge(var_made, b * TILES + (h * QT + t + 1))
                    pool.tensor_tensor(rstd[:, :], var_eps[:, :], minus_half[:, 0:1], ALU.pow).then_inc(rstd_made, 1)

            def batch(b):
                for h in range(HALVES):
                    sums(b, h)
                    powers(b, h)

            with pool.Fori(0, B) as b:
                batch(b)


def kernel(x, adj, L0_gnn_Wq, L0_gnn_Wk, L0_gnn_Wv):
    import numpy as np
    import concourse.bacc as bacc
    from concourse.bass_utils import run_bass_kernel_spmd

    x = np.ascontiguousarray(x)
    arrays = {
        "x": x,
        "xT": np.ascontiguousarray(x.transpose(0, 2, 1)),
        "adj": np.ascontiguousarray(adj),
        "wq": np.ascontiguousarray(L0_gnn_Wq),
        "wk": np.ascontiguousarray(L0_gnn_Wk),
        "wvT": np.ascontiguousarray(np.asarray(L0_gnn_Wv).T),
    }
    nc = bacc.Bacc("TRN2", target_bir_lowering=False, num_devices=1)
    args = [nc.dram_tensor(name, a.shape, mybir.dt.from_np(a.dtype), kind="ExternalInput").ap()
            for name, a in arrays.items()]
    out = nc.dram_tensor("out", x.shape, mybir.dt.from_np(x.dtype), kind="ExternalOutput").ap()
    adjacency_attention_layernorm(nc, *args, out)
    result = run_bass_kernel_spmd(nc, [arrays], core_ids=[0])
    return result.results[0]["out"]
```

```python
from contextlib import ExitStack

import concourse.bass as bass
from concourse import mybir

F32 = mybir.dt.float32
F32R = mybir.dt.float32r
ALU = mybir.AluOpType
ACT = mybir.ActivationFunctionType
AX = mybir.AxisListType

P = 128
BANK = 512
DMA = 16
EPS = 1e-5


def adjacency_attention_layernorm(nc, x, xT, adj, wq, wk, wvT, out):
    B, N, D = x.shape
    KD = D // P
    MT = N // P
    HALVES = N // BANK
    QT = BANK // P
    Q = 32
    assert D == BANK and HALVES == 2 and KD == QT == 4

    FIRST_GROUPS = KD + MT
    GROUPS = KD + QT + KD + QT + MT
    Y1, O0, Y0, O1, V = 0, KD, KD + QT, 2 * KD + QT, 2 * KD + 2 * QT
    SPLITS = KD + KD + MT
    SPLIT_Y1, SPLIT_Y0, SPLIT_V = 0, KD, 2 * KD
    O1_LAST = Y0
    SCORES = HALVES * MT
    PIECES = HALVES * KD
    TILES = HALVES * QT
    RING = 3
    SRING = 4
    MRING = 2
    SQRING = 2
    COPIES = (P // Q) ** 2
    assert GROUPS % RING == 0 and SCORES % SRING == 0

    with ExitStack() as ctx:
        def sb(name, shape, dt):
            return ctx.enter_context(nc.sbuf_tensor(name, shape, dt))

        def sem(name):
            return ctx.enter_context(nc.semaphore(name))

        x_hi = sb("x_hi", [P, KD, N], F32R)
        x_lo = sb("x_lo", [P, KD, N], F32R)
        x_raw = sb("x_raw", [P, KD, BANK], F32)
        a_hi = sb("a_hi", [P, KD, D], F32R)
        a_lo = sb("a_lo", [P, KD, D], F32R)
        wv_hi = sb("wv_hi", [P, KD, D], F32R)
        wv_lo = sb("wv_lo", [P, KD, D], F32R)
        y_hi = sb("y_hi", [P, KD, BANK], F32R)
        y_lo = sb("y_lo", [P, KD, BANK], F32R)
        v_hi = sb("v_hi", [P, MT, D], F32R)
        v_lo = sb("v_lo", [P, MT, D], F32R)
        rel_hi = sb("rel_hi", [P, MT, BANK], F32R)
        rel_lo = sb("rel_lo", [P, MT, BANK], F32R)
        adj_sb = sb("adj_sb", [P, MT, N], F32)
        masked = sb("masked", [P, MRING, BANK], F32)
        squares = sb("squares", [P, SQRING, BANK], F32)
        square_sum = sb("square_sum", [P, BANK], F32)
        blocks_t = sb("blocks_t", [P, BANK], F32)
        block_sums = sb("block_sums", [P, BANK // Q], F32)
        quad_sums = sb("quad_sums", [P, QT, P // Q], F32)
        res = sb("res", [P, QT, D], F32)
        minus_half = sb("minus_half", [P, QT], F32)
        norm2 = sb("norm2", [P, QT], F32)
        rnorm = sb("rnorm", [P, QT], F32)
        stats = sb("stats", [P, 6], F32)
        mean_var = sb("mean_var", [P, 2], F32)
        var_eps = sb("var_eps", [P, 1], F32)
        rstd = sb("rstd", [P, 1], F32)

        ring = [ctx.enter_context(nc.psum_tensor(f"ring{i}", [P, BANK], F32)) for i in range(RING)]
        score = [ctx.enter_context(nc.psum_tensor(f"score{i}", [P, BANK], F32)) for i in range(SRING)]

        wqk_loaded = [sem(f"wqk_loaded{k}") for k in range(KD)]
        wv_loaded = sem("wv_loaded")
        x_loaded = sem("x_loaded")
        adj_loaded = [sem(f"adj_loaded{h}") for h in range(HALVES)]
        res_loaded = sem("res_loaded")
        out_stored = sem("out_stored")
        const_set = sem("const_set")
        w_hi_made = sem("w_hi_made")
        w_split = sem("w_split")
        a_done = sem("a_done")
        a_hi_made = sem("a_hi_made")
        a_split = sem("a_split")
        x_hi_made = sem("x_hi_made")
        x_split = sem("x_split")
        group_done = sem("group_done")
        group_hi_made = sem("group_hi_made")
        group_taken = sem("group_taken")
        score_done = sem("score_done")
        score_masked = sem("score_masked")
        rel_hi_made = sem("rel_hi_made")
        rel_split = sem("rel_split")
        squared = sem("squared")
        square_added = sem("square_added")
        blocks_turned = sem("blocks_turned")
        blocks_summed = sem("blocks_summed")
        quads_placed = sem("quads_placed")
        norm2_made = sem("norm2_made")
        rnorm_made = sem("rnorm_made")
        mean_var_made = sem("mean_var_made")
        var_made = sem("var_made")
        rstd_made = sem("rstd_made")
        normed = sem("normed")

        w_stage = adj_sb[:, :, :].rearrange("p m (a n) -> p (m a) n", n=BANK)
        wq_raw, wk_raw, wv_raw = (w_stage[:, KD * i:KD * (i + 1), :] for i in range(3))
        wq_hi, wq_lo = rel_hi[:, 0:KD, :], rel_lo[:, 0:KD, :]
        wk_hi, wk_lo = rel_hi[:, KD:2 * KD, :], rel_lo[:, KD:2 * KD, :]
        wqk = [(wq_raw, wq_hi, wq_lo), (wk_raw, wk_hi, wk_lo)]
        weight_pieces = [tuple(a[:, k, :] for a in w) for k in range(KD) for w in wqk]
        weight_pieces += [(wv_raw[:, k, :], wv_hi[:, k, :], wv_lo[:, k, :]) for k in range(KD)]

        xT_v = xT.rearrange("b (k p) n -> b p k n", p=P)
        x_v = x.rearrange("b (t p) d -> b p t d", p=P)
        out_v = out.rearrange("b (t p) d -> b p t d", p=P)
        adj_v = adj.rearrange("(m p) n -> p m n", p=P)

        def w_v(w):
            return w.rearrange("(k p) d -> p k d", p=P)

        def half(h):
            return slice(h * BANK, (h + 1) * BANK)

        def group_index(b, g):
            return b * GROUPS + (FIRST_GROUPS + g)

        def added_before(b, h):
            return b * (HALVES * (MT - 1)) + (h + 1) * (MT - 1)

        def first_target(g):
            if g < QT:
                return v_hi[:, g, :], v_lo[:, g, :]
            if g < QT + KD:
                return y_hi[:, g - QT, :], y_lo[:, g - QT, :]
            return v_hi[:, g - KD, :], v_lo[:, g - KD, :]

        def bank(g):
            return ring[(FIRST_GROUPS + g) % RING]

        block = ctx.enter_context(nc.Block())

        @block.sync
        def _(sp):
            for k in range(KD):
                sp.dma_start(wq_raw[:, k, :], w_v(wq)[:, k, :]).then_inc(wqk_loaded[k], DMA)
                sp.dma_start(wk_raw[:, k, :], w_v(wk)[:, k, :]).then_inc(wqk_loaded[k], DMA)
            sp.dma_start(x_raw[:, :, :], xT_v[0, :, :, half(0)]).then_inc(x_loaded, DMA)
            sp.dma_start(wv_raw, w_v(wvT)).then_inc(wv_loaded, DMA)
            sp.wait_ge(x_split, KD)
            sp.dma_start(x_raw[:, :, :], xT_v[0, :, :, half(1)]).then_inc(x_loaded, DMA)
            sp.wait_ge(w_split, 3 * KD)
            for h in range(HALVES):
                sp.dma_start(adj_sb[:, :, half(h)], adj_v[:, :, half(h)]).then_inc(adj_loaded[h], DMA)

            def load_x(b, h):
                sp.wait_ge(x_split, b * PIECES + h * KD)
                sp.dma_start(x_raw[:, :, :], xT_v[b, :, :, half(h)]).then_inc(x_loaded, DMA)

            def load_res(b, h):
                sp.dma_start(res[:, :, :], x_v[b, :, h * QT:(h + 1) * QT, :]).then_inc(res_loaded, DMA)

            def store(b, h):
                for t in range(QT):
                    sp.wait_ge(normed, b * TILES + (h * QT + t + 1))
                    sp.dma_start(out_v[b, :, h * QT + t, :], res[:, t, :]).then_inc(out_stored, DMA)
                sp.wait_ge(out_stored, b * (TILES * DMA) + (h + 1) * QT * DMA)

            def batch(b, last):
                if not last:
                    load_x(b + 1, 0)
                store(b, 0)
                load_res(b, 1)
                if not last:
                    load_x(b + 1, 1)
                store(b, 1)
                if not last:
                    load_res(b + 1, 0)

            load_res(0, 0)
            with sp.Fori(0, B - 1) as b:
                batch(b, False)
            batch(B - 1, True)

        @block.tensor
        def _(pe):
            def product(bank_ap, pairs, ready=None):
                for i, ((l_hi, l_lo), (r_hi, r_lo)) in enumerate(pairs):
                    if ready:
                        pe.wait_ge(*ready[i])
                    pe.matmul(bank_ap, l_hi, r_hi, start=(i == 0), stop=False)
                    pe.matmul(bank_ap, l_hi, r_lo, start=False, stop=False)
                    mm = pe.matmul(bank_ap, l_lo, r_hi, start=False, stop=(i == len(pairs) - 1))
                return mm

            def tile_of(hi, lo, k, cols):
                return hi[:, k, cols], lo[:, k, cols]

            def cols(i):
                return slice(i * P, (i + 1) * P)

            def y_group(j, h, bank_ap):
                return product(bank_ap, [(tile_of(a_hi, a_lo, k, cols(j)), tile_of(x_hi, x_lo, k, half(h)))
                                         for k in range(KD)])

            def v_group(m, bank_ap):
                return product(bank_ap, [(tile_of(x_hi, x_lo, k, cols(m)), tile_of(wv_hi, wv_lo, k, slice(0, D)))
                                         for k in range(KD)])

            for k in range(KD):
                pe.wait_ge(w_split, 2 * k + 2)
                for j in range(KD):
                    bank_ap = score[j][:]
                    l_hi, l_lo = tile_of(wq_hi, wq_lo, k, cols(j))
                    pe.matmul(bank_ap, l_hi, wk_hi[:, k, :], start=(k == 0), stop=False)
                    pe.matmul(bank_ap, l_hi, wk_lo[:, k, :], start=False, stop=False)
                    mm = pe.matmul(bank_ap, l_lo, wk_hi[:, k, :], start=False, stop=(k == KD - 1))
                    if k == KD - 1:
                        mm.then_inc(a_done, 1)
            for g in range(FIRST_GROUPS):
                if g == 0:
                    pe.wait_ge(x_split, KD)
                    pe.wait_ge(w_split, 3 * KD)
                if g >= RING:
                    pe.wait_ge(group_taken, g - RING + 1)
                if g < QT:
                    mm = v_group(g, ring[g % RING][:])
                elif g < QT + KD:
                    if g == QT:
                        pe.wait_ge(a_split, KD)
                    mm = y_group(g - QT, 0, ring[g % RING][:])
                else:
                    if g == QT + KD:
                        pe.wait_ge(x_split, PIECES)
                    mm = v_group(g - KD, ring[g % RING][:])
                mm.then_inc(group_done, 1)
            def free_bank(b, g):
                pe.wait_ge(group_taken, group_index(b, g) - RING + 1)

            def scores(b, h):
                for i in range(MT):
                    s = h * MT + i
                    pe.wait_ge(score_masked, b * SCORES + (s + 1))
                    product(score[s % SRING][:], [(tile_of(x_hi, x_lo, k, cols(i)), tile_of(y_hi, y_lo, k, slice(0, BANK)))
                                                  for k in range(KD)]).then_inc(score_done, 1)

            def outputs(b, h, g0, at_once):
                pe.wait_ge(group_taken, group_index(b, 0))
                for t in range(QT):
                    free_bank(b, g0 + t)
                    ready = None
                    if t == 0 and at_once:
                        ready = [(rel_split, b * SCORES + (h * MT + m + 1 + MRING)) for m in range(MT)]
                    elif t == 0:
                        pe.wait_ge(rel_split, b * SCORES + ((h + 1) * MT + MRING))
                    product(bank(g0 + t)[:], [(tile_of(rel_hi, rel_lo, m, cols(t)), tile_of(v_hi, v_lo, m, slice(0, D)))
                                              for m in range(MT)], ready).then_inc(group_done, 1)

            def batch(b, last):
                pe.wait_ge(group_taken, group_index(b, -QT))
                scores(b, 0)
                for j in range(KD):
                    free_bank(b, Y1 + j)
                    y_group(j, 1, bank(Y1 + j)[:]).then_inc(group_done, 1)
                outputs(b, 0, O0, False)
                pe.wait_ge(group_taken, group_index(b, Y1 + KD))
                scores(b, 1)
                if not last:
                    for j in range(KD):
                        if j == 0:
                            pe.wait_ge(x_split, (b + 1) * PIECES + KD)
                        free_bank(b, Y0 + j)
                        y_group(j, 0, bank(Y0 + j)[:]).then_inc(group_done, 1)
                outputs(b, 1, O1 if not last else O1_LAST, last)
                if not last:
                    for m in range(MT):
                        if m == QT:
                            pe.wait_ge(x_split, (b + 2) * PIECES)
                        free_bank(b, V + m)
                        v_group(m, bank(V + m)[:]).then_inc(group_done, 1)

            with nc.Fori(0, B - 1, engines=[pe.engine], hint_back_edge=True) as b:
                batch(b, False)
            batch(B - 1, True)

        @block.scalar
        def _(act):
            def x_piece(b, h, k):
                if k == 0:
                    act.wait_ge(x_loaded, b * (HALVES * DMA) + (h + 1) * DMA)
                act.activation(x_hi[:, k, half(h)], x_raw[:, k, :], ACT.Copy).then_inc(x_hi_made, 1)

            def group(ap_hi, g_index, bank_ap):
                act.wait_ge(group_done, g_index + 1)
                act.activation(ap_hi, bank_ap[:], ACT.Copy).then_inc(group_hi_made, 1)

            for i, (raw, hi, _) in enumerate(weight_pieces):
                if i < 2 * KD and i % 2 == 0:
                    act.wait_ge(wqk_loaded[i // 2], 2 * DMA)
                if i == 2 * KD:
                    for k in range(KD):
                        x_piece(0, 0, k)
                    act.wait_ge(wv_loaded, DMA)
                act.activation(hi, raw, ACT.Copy).then_inc(w_hi_made, 1)
            for j in range(KD):
                act.wait_ge(a_done, j + 1)
                act.activation(a_hi[:, j, :], score[j][:], ACT.Copy).then_inc(a_hi_made, 1)
            for g in range(FIRST_GROUPS):
                if g == QT:
                    for k in range(KD):
                        x_piece(0, 1, k)
                group(first_target(g)[0], g, ring[g % RING])

            def scores(b, h, last):
                for i in range(MT):
                    s = h * MT + i
                    act.wait_ge(score_masked, b * SCORES + (s + 1 + SRING))
                    act.activation(rel_hi[:, i, :], masked[:, s % MRING, :], ACT.Copy).then_inc(rel_hi_made, 1)
                    if i == 0:
                        act.wait_ge(blocks_turned, b * HALVES + (h + 1))
                        sq = square_sum[:, :]
                    else:
                        act.wait_ge(square_added, added_before(b, h) + max(i - SQRING, 0))
                        sq = squares[:, i % SQRING, :]
                    act.activation(sq, masked[:, s % MRING, :], ACT.Square).then_inc(squared, 1)
                    if h == 1 and not last and KD <= i < KD + 2:
                        x_piece(b + 1, 0, 2 * (i - KD))
                        x_piece(b + 1, 0, 2 * (i - KD) + 1)

            def batch(b, last):
                scores(b, 0, last)
                for j in range(KD):
                    group(y_hi[:, j, :], group_index(b, Y1 + j), bank(Y1 + j))
                scores(b, 1, last)
                if not last:
                    for j in range(KD):
                        group(y_hi[:, j, :], group_index(b, Y0 + j), bank(Y0 + j))
                    for k in range(KD):
                        x_piece(b + 1, 1, k)
                    for m in range(MT):
                        group(v_hi[:, m, :], group_index(b, V + m), bank(V + m))

            with act.Fori(0, B - 1) as b:
                batch(b, False)
            batch(B - 1, True)

        @block.vector
        def _(dve):
            def x_piece(b, h, k):
                dve.wait_ge(x_hi_made, b * PIECES + (h * KD + k + 1))
                dve.tensor_tensor(x_lo[:, k, half(h)], x_raw[:, k, :], x_hi[:, k, half(h)].bitcast(F32),
                                  ALU.subtract).then_inc(x_split, 1)

            def group(ap_hi, ap_lo, hi_count, bank_ap):
                dve.wait_ge(group_hi_made, hi_count)
                dve.tensor_tensor(ap_lo, bank_ap[:], ap_hi.bitcast(F32), ALU.subtract).then_inc(group_taken, 1)

            for i, (raw, hi, lo) in enumerate(weight_pieces):
                if i == 2 * KD:
                    for k in range(KD):
                        x_piece(0, 0, k)
                dve.wait_ge(w_hi_made, i + 1)
                dve.tensor_tensor(lo, raw, hi.bitcast(F32), ALU.subtract).then_inc(w_split, 1)
            for j in range(KD):
                dve.wait_ge(a_hi_made, j + 1)
                dve.tensor_tensor(a_lo[:, j, :], score[j][:], a_hi[:, j, :].bitcast(F32),
                                  ALU.subtract).then_inc(a_split, 1)
            for g in range(FIRST_GROUPS):
                if g == QT:
                    for k in range(KD):
                        x_piece(0, 1, k)
                group(*first_target(g), g + 1, ring[g % RING])

            def loop_group(b, ap_hi, ap_lo, split, g):
                group(ap_hi, ap_lo, b * SPLITS + (FIRST_GROUPS + split + 1), bank(g))

            def rest_of_scores(b, h, i):
                s = h * MT + i
                dve.wait_ge(rel_hi_made, b * SCORES + (s + 1))
                dve.tensor_tensor(rel_lo[:, i, :], masked[:, s % MRING, :], rel_hi[:, i, :].bitcast(F32),
                                  ALU.subtract).then_inc(rel_split, 1)

            def scores(b, h, last):
                dve.wait_ge(adj_loaded[h], DMA)
                for i in range(MT):
                    s = h * MT + i
                    dve.wait_ge(score_done, b * SCORES + (s + 1))
                    dve.wait_ge(squared, b * SCORES + (s + 1))
                    dve.wait_ge(rel_split, b * SCORES + (s + 1))
                    dve.tensor_tensor(masked[:, s % MRING, :], score[s % SRING][:], adj_sb[:, i, half(h)],
                                      ALU.mult).then_inc(score_masked, 1)
                    if i > 0:
                        rest_of_scores(b, h, i - 1)
                    if h == 1 and not last and KD < i <= KD + 2:
                        x_piece(b + 1, 0, 2 * (i - KD - 1))
                        x_piece(b + 1, 0, 2 * (i - KD - 1) + 1)
                rest_of_scores(b, h, MT - 1)

            def norms(b, h):
                n = b * HALVES + h
                dve.wait_ge(square_added, added_before(b, h + 1))
                dve.transpose(blocks_t[:, :], square_sum[:, :]).then_inc(blocks_turned, 1)
                dve.wait_ge(blocks_turned, n + 2)
                dve.tensor_reduce(block_sums[:, :], blocks_t[:, :].rearrange("p (c q) -> p c q", q=Q),
                                  AX.X, ALU.add).then_inc(blocks_summed, 1)
                dve.wait_ge(blocks_summed, n + 1)
                for to in range(P // Q):
                    for of in range(P // Q):
                        dve.tensor_copy(quad_sums[Q * to:Q * (to + 1), :, of],
                                        block_sums[Q * of:Q * (of + 1), to::P // Q]).then_inc(quads_placed, 1)
                dve.wait_ge(quads_placed, b * (HALVES * COPIES) + (h + 1) * COPIES)
                dve.tensor_reduce(norm2[:, :], quad_sums[:, :, :], AX.X, ALU.add).then_inc(norm2_made, 1)

            def outputs(b, h, g0, next_x):
                norms(b, h)
                dve.wait_ge(res_loaded, b * (HALVES * DMA) + (h + 1) * DMA)
                dve.wait_ge(rnorm_made, b * HALVES + (h + 1))
                for t in range(QT):
                    tile = b * TILES + (h * QT + t)
                    dve.wait_ge(group_done, group_index(b, g0 + t + 1))
                    dve.scalar_tensor_tensor(out=res[:, t, :], in0=bank(g0 + t)[:], scalar=rnorm[:, t:t + 1],
                                             in1=res[:, t, :], op0=ALU.mult, op1=ALU.add).then_inc(group_taken, 1)
                    dve.wait_ge(group_taken, group_index(b, g0 + t + 1))
                    dve.bn_stats(stats[:, :], res[:, t, :])
                    dve.drain()
                    dve.bn_aggr(mean_var[:, :], stats[:, :]).then_inc(mean_var_made, 1)
                    dve.wait_ge(mean_var_made, tile + 1)
                    dve.tensor_scalar(var_eps[:, :], mean_var[:, 1:2], EPS, None, ALU.add).then_inc(var_made, 1)
                    dve.wait_ge(rstd_made, tile + 1)
                    dve.tensor_scalar(res[:, t, :], res[:, t, :], mean_var[:, 0:1], rstd[:, 0:1],
                                      ALU.subtract, ALU.mult).then_inc(normed, 1)
                    if next_x:
                        x_piece(b + 1, 1, t)

            def batch(b, last):
                scores(b, 0, last)
                for j in range(KD):
                    loop_group(b, y_hi[:, j, :], y_lo[:, j, :], SPLIT_Y1 + j, Y1 + j)
                outputs(b, 0, O0, False)
                scores(b, 1, last)
                if not last:
                    for j in range(KD):
                        loop_group(b, y_hi[:, j, :], y_lo[:, j, :], SPLIT_Y0 + j, Y0 + j)
                outputs(b, 1, O1 if not last else O1_LAST, not last)
                if not last:
                    for m in range(MT):
                        loop_group(b, v_hi[:, m, :], v_lo[:, m, :], SPLIT_V + m, V + m)

            with dve.Fori(0, B - 1) as b:
                batch(b, False)
            batch(B - 1, True)

        @block.gpsimd
        def _(pool):
            pool.memset(minus_half[:, :], -0.5).then_inc(const_set, 1)
            pool.sem_inc(score_masked, SRING)
            pool.sem_inc(squared, MRING)
            pool.sem_inc(rel_split, MRING)
            pool.sem_inc(square_added, MT - 1)
            pool.sem_inc(blocks_turned, 1)
            pool.wait_ge(const_set, 1)

            def sums(b, h):
                for i in range(1, MT):
                    pool.wait_ge(squared, b * SCORES + (h * MT + i + 1 + MRING))
                    pool.wait_ge(square_added, added_before(b, h) + (i - 1))
                    pool.tensor_tensor(square_sum[:, :], square_sum[:, :], squares[:, i % SQRING, :],
                                       ALU.add).then_inc(square_added, 1)

            def powers(b, h):
                pool.wait_ge(norm2_made, b * HALVES + (h + 1))
                pool.tensor_tensor(rnorm[:, :], norm2[:, :], minus_half[:, :], ALU.pow).then_inc(rnorm_made, 1)
                for t in range(QT):
                    pool.wait_ge(var_made, b * TILES + (h * QT + t + 1))
                    pool.tensor_tensor(rstd[:, :], var_eps[:, :], minus_half[:, 0:1], ALU.pow).then_inc(rstd_made, 1)

            def batch(b):
                for h in range(HALVES):
                    sums(b, h)
                    powers(b, h)

            with pool.Fori(0, B) as b:
                batch(b)


def kernel(x, adj, L0_gnn_Wq, L0_gnn_Wk, L0_gnn_Wv):
    import numpy as np
    import concourse.bacc as bacc
    from concourse.bass_utils import run_bass_kernel_spmd

    x = np.ascontiguousarray(x)
    arrays = {
        "x": x,
        "xT": np.ascontiguousarray(x.transpose(0, 2, 1)),
        "adj": np.ascontiguousarray(adj),
        "wq": np.ascontiguousarray(L0_gnn_Wq),
        "wk": np.ascontiguousarray(L0_gnn_Wk),
        "wvT": np.ascontiguousarray(np.asarray(L0_gnn_Wv).T),
    }
    nc = bacc.Bacc("TRN2", target_bir_lowering=False, num_devices=1)
    args = [nc.dram_tensor(name, a.shape, mybir.dt.from_np(a.dtype), kind="ExternalInput").ap()
            for name, a in arrays.items()]
    out = nc.dram_tensor("out", x.shape, mybir.dt.from_np(x.dtype), kind="ExternalOutput").ap()
    adjacency_attention_layernorm(nc, *args, out)
    result = run_bass_kernel_spmd(nc, [arrays], core_ids=[0])
    return result.results[0]["out"]
```
